# Optimizing a Trainium2 kernel written in Bass

```python
import numpy as np
import jax
import jax.numpy as jnp

def _softmax(x, axis=-1):
    return jax.nn.softmax(x, axis=axis)
def _gelu(x):
    return jax.nn.gelu(x, approximate=True)
def _silu(x):
    return jax.nn.silu(x)
def _sigmoid(x):
    return jax.nn.sigmoid(x)
def _layernorm(x, axis=-1, eps=1e-5):
    m = jnp.mean(x, axis=axis, keepdims=True)
    v = jnp.var(x, axis=axis, keepdims=True)
    return (x - m) / jnp.sqrt(v + eps)
def _scatter_add(tgt, idx, src, axis=0):
    return tgt.at[idx].add(src)
def _segment_sum(src, seg, n):
    return jax.ops.segment_sum(src, seg, n)

kernel_name = 'mk_adj_resnorm_d1_adj_256_233329'

def setup_inputs(seed: int = 0):
    np.random.seed(seed)
    _w = jnp.asarray
    def _rec_inputs():
        import jax
        import jax.numpy as jnp
        _gk = jax.random.key(seed)
        x = -0.0005207 + 1.001 * jax.random.normal(jax.random.fold_in(_gk, 1), (8, 2048, 256), jnp.float32)
        _a = jax.random.bernoulli(jax.random.fold_in(_gk, 2), 0.0078125, (8, 2048, 2048))
        _a = jnp.logical_or(_a, jnp.swapaxes(_a, -1, -2))
        _a = jnp.logical_or(_a, jnp.eye(2048, dtype=bool))
        _af = _a.astype(jnp.float32)
        _af = _af * jax.random.uniform(jax.random.fold_in(_gk, 3), (8, 2048, 2048), jnp.float32, 0.05, 1)
        adj = _af
        return x, adj
    x, adj = _rec_inputs()
    def _L0_gnn_setup():
        import math
        import jax, jax.numpy as jnp
        import numpy as np
        HIDDEN = 256
        HEADS = 8
        HEAD_DIM = HIDDEN // HEADS
        key = jax.random.key(seed)
        ks = jax.random.split(key, 8)
        b, n = (2, 4096)
        node_state = jax.random.normal(ks[0], (b, n, HIDDEN), dtype=jnp.float32)
        adjacency = jax.random.uniform(ks[1], (b, n, n), dtype=jnp.float32)
        s = 1.0 / math.sqrt(HIDDEN)
        Wq = jax.random.uniform(ks[2], (HIDDEN, HIDDEN), jnp.float32, -s, s)
        Wk = jax.random.uniform(ks[3], (HIDDEN, HIDDEN), jnp.float32, -s, s)
        Wv = jax.random.uniform(ks[4], (HIDDEN, HIDDEN), jnp.float32, -s, s)
        Wo = jax.random.uniform(ks[5], (HIDDEN, HIDDEN), jnp.float32, -s, s)
        bo = jax.random.uniform(ks[6], (HIDDEN,), jnp.float32, -s, s)
        return {'node_state': node_state, 'adjacency': adjacency, 'Wq': Wq, 'Wk': Wk, 'Wv': Wv, 'Wo': Wo, 'bo': bo}
    _L0_gnn_all = _L0_gnn_setup()
    _L0_gnn_in = {k: v for k, v in _L0_gnn_all.items() if k in ('Wq', 'Wk', 'Wv', 'Wo', 'bo', )}
    del _L0_gnn_all

    return {
        "x": x,
        "adj": adj,
        "L0_gnn_Wq": _L0_gnn_in["Wq"],
        "L0_gnn_Wk": _L0_gnn_in["Wk"],
        "L0_gnn_Wv": _L0_gnn_in["Wv"],
        "L0_gnn_Wo": _L0_gnn_in["Wo"],
        "L0_gnn_bo": _L0_gnn_in["bo"],
    }

def reference(x, adj, L0_gnn_Wq, L0_gnn_Wk, L0_gnn_Wv, L0_gnn_Wo, L0_gnn_bo):
    import jax
    import jax.numpy as jnp
    def _L0_gnn_ref(node_state, adjacency, Wq, Wk, Wv, Wo, bo):
        import math
        import jax, jax.numpy as jnp
        import numpy as np
        HIDDEN = 256
        HEADS = 8
        HEAD_DIM = HIDDEN // HEADS
        b, n, _ = node_state.shape

        def split_heads(x):
            return x.reshape(b, n, HEADS, HEAD_DIM).transpose(0, 2, 1, 3)
        q = split_heads(node_state @ Wq.T)
        k = split_heads(node_state @ Wk.T)
        v = split_heads(node_state @ Wv.T)
        scores = jnp.einsum('bhqd,bhkd->bhqk', q, k) / math.sqrt(HEAD_DIM)
        log_adj = jnp.log(adjacency + 1e-06)
        scores = scores + log_adj[:, None, :, :]
        attn = jax.nn.softmax(scores, axis=-1)
        out = jnp.einsum('bhqk,bhkd->bhqd', attn, v)
        out = out.transpose(0, 2, 1, 3).reshape(b, n, HIDDEN)
        return out @ Wo.T + bo

    x = _layernorm(x + _L0_gnn_ref(x, adj, L0_gnn_Wq, L0_gnn_Wk, L0_gnn_Wv, L0_gnn_Wo, L0_gnn_bo), axis=-1)
    return x


_drawn_inputs = setup_inputs


def setup_inputs(seed=0):
    import zlib

    import numpy as np

    out = dict(_drawn_inputs(seed))
    spreads = {}
    factors = {}
    for name, (base, spread) in spreads.items():
        noise = np.random.default_rng([zlib.crc32(name.encode()), seed]).standard_normal(out[name].shape)
        drawn = base * np.exp(spread * noise) if base else spread * noise
        out[name] = jnp.asarray(drawn.astype(out[name].dtype))
    for name, factor in factors.items():
        out[name] = (out[name] * factor).astype(out[name].dtype)
    return out
```

```python
from contextlib import ExitStack

import concourse.bass as bass
from concourse import mybir

P = 128
F32 = mybir.dt.float32
F16 = mybir.dt.float16
ALU = mybir.AluOpType
ACT = mybir.ActivationFunctionType
AX_X = mybir.AxisListType.X

B, N, D, H = 8, 2048, 256, 8
HD = D // H
QC = 512
NC = N // QC
QT = QC // P
KT = N // P
HG = H // 4
NPASS = NC * HG
NU = NPASS * KT
DT = D // P
SCALE = float(HD) ** -0.5
ADJ_EPS = 1e-6
LN_EPS = 1e-5
KROWS = 3 * HD
SROWS = KROWS + 2
RING = 4
QRING = 4
MAXP = 4 * QT * (N // 512)
MAX_AT = 12
HA = 1
LEAD = 16
LOOK = 2


def aux_items(j, u, skip_next):
    c, g = divmod(j, HG)
    items = []
    if j >= 1 and u == 1:
        items.append(("den_t", j - 1))
    if j >= 1 and u == 3:
        items.append(("rden", j - 1))
    if j >= 2 and g == 0 and 5 <= u < 5 + QT:
        items.append(("proj", c - 1, u - 5))
    if j == 0 and u < MAX_AT:
        items += [("max", 1, p) for p in range(MAXP) if p * MAX_AT // MAXP == u]
    k = j + 1 if u < MAX_AT else j + 2
    if 2 <= k <= NPASS and not (skip_next and k == NPASS):
        at = (u - MAX_AT) % KT
        items += [("max", k, p) for p in range(MAXP) if p * KT // MAXP == at]
    if u == MAX_AT and not (skip_next and j == NPASS - 1):
        items.append(("max_t", j + 1))
    if u % 2 == 0 and not (skip_next and c == NC - 1):
        items.append(("adj_t", c + 1, g * (KT // 2) + u // 2))
    return items


def tail_items():
    return [("den_t", NPASS - 1), ("rden", NPASS - 1)] + [("proj", NC - 1, t) for t in range(QT)]


def prologue_items():
    items = []
    for kt in range(KT):
        items += [("max", 0, p) for p in range(kt * MAXP // KT, (kt + 1) * MAXP // KT)]
        items.append(("adj_t", 0, kt))
    return items + [("max_t", 0)]


def attention_layer(nc, x, adj, wq, wk, wv, wo, bo, out):
    ctx = ExitStack()
    with ctx:
        def sb(name, shape, dt):
            return ctx.enter_context(nc.sbuf_tensor(name, shape, dt))

        def sem(name):
            return ctx.enter_context(nc.semaphore(name))

        parts = nc.dram_tensor("qk_parts", [4, B * D, N], F16, kind="Internal").ap()
        QHI, QLO, KHI, KLO = range(4)
        v_rows = nc.dram_tensor("v_rows", [B * N, D], F32, kind="Internal").ap()

        ident = sb("ident", [P, P], F32)
        ones_v = sb("ones_v", [P, HD], F32)
        wT = sb("wT", [P, 4, DT, D], F32)
        bo_b = sb("bo_b", [P, D], F32)
        minus_half = sb("minus_half", [P, QT], F32)
        adjT = sb("adjT", [P, 2, KT, QC], F32)
        adj_nat = sb("adj_nat", [P, 2, QT, 2 * P], F32)
        kmain = sb("kmain", [SROWS, 2, 4, N], F16)
        kext = sb("kext", [SROWS, 4, N], F16)
        vmain = sb("vmain", [P, 2, KT, P], F32)
        qst = sb("qst", [SROWS, QRING, 4, QC], F16)
        pa = sb("pa", [P, RING, HA, QC], F32)
        pb = sb("pb", [P, RING, 4 - HA, QC], F32)
        mpart = sb("mpart", [P, 2, MAXP], F32)
        m16 = sb("m16", [P, 4 * QT], F32)
        mrow = sb("mrow", [4 * QT, 2, P], F16)
        den_s = sb("den_s", [P, QC], F32)
        rcp = sb("rcp", [P, QT, 4], F32)
        rcp32 = sb("rcp32", [P, QT, 4, HD], F32)
        attnT = sb("attnT", [P, HG, QC], F32)
        y = sb("y", [P, QT, D], F32)
        stats = sb("stats", [P, QT, 6], F32)
        mv = sb("mv", [P, 7, QT], F32)
        rstd = sb("rstd", [P, QT], F32)
        nmean = sb("nmean", [P, QT], F32)

        flat = adjT[:, :, :, :].rearrange("p a k q -> p (a k q)")
        W = QT * D
        x_in = flat[:, 0:2 * W].rearrange("p (s t d) -> p s t d", s=2, t=QT)
        xT = flat[:, 2 * W:4 * W].rearrange("p (s k q) -> p s k q", s=2, k=DT)
        v_st = flat[:, 4 * W:6 * W].rearrange("p (s t d) -> p s t d", s=2, t=QT)
        hi_st = flat[:, 6 * W:8 * W].bitcast(F16).rearrange("p (s f q) -> p s f q", s=2, f=4)
        lo_st = flat[:, 8 * W:10 * W].bitcast(F16).rearrange("p (s f q) -> p s f q", s=2, f=4)
        w_in = flat[:, 10 * W:12 * W].rearrange("p (w o d) -> p w o d", w=4, o=DT)

        ps = ctx.enter_context(nc.psum_tensor("ps", [P, 8, 512], F32))
        sc_b = ps[:, 0:4 - HA, :]
        sc_a = ps[:, 4 - HA:4, :]
        pv_ps = ps[:, 4, :]
        den_ps = ps[:, 5, :]

        def aux(n):
            return ps[:, 6 + n % 2, :]

        w_ready = sem("w_ready"); bo_ready = sem("bo_ready")
        const_ready = sem("const_ready"); ident_zero = sem("ident_zero")
        wT_ps = sem("wT_ps"); wT_done = sem("wT_done")
        x_ready = [sem("x_ready0"), sem("x_ready1")]
        xT_ps = sem("xT_ps"); xT_done = sem("xT_done")
        qk_ps = sem("qk_ps"); hi_done = sem("hi_done"); lo_done = sem("lo_done")
        v_ps = sem("v_ps"); v_done = sem("v_done")
        hi_stored = [sem("hi_stored0"), sem("hi_stored1")]
        lo_stored = [sem("lo_stored0"), sem("lo_stored1")]
        v_stored = [sem("v_stored0"), sem("v_stored1")]

        k_ready = [sem("k_ready0"), sem("k_ready1")]; kext_ready = sem("kext_ready")
        v_ready = [sem("v_ready0"), sem("v_ready1")]
        q_ready = [sem(f"q_ready{i}") for i in range(QRING)]
        mrow_in = [sem("mrow_in0"), sem("mrow_in1")]
        adj_in = [sem("adj_in0"), sem("adj_in1")]
        xres_in = sem("xres_in"); out_done = sem("out_done")
        st_a = sem("st_a"); st_b = sem("st_b")
        exp_a = sem("exp_a"); exp_b = sem("exp_b")
        mul_a = sem("mul_a"); mul_b = sem("mul_b")
        pv_done = sem("pv_done")
        evac = sem("evac")
        max_mm = sem("max_mm"); max_red = sem("max_red")
        m_ready = sem("m_ready"); maxt_mm = sem("maxt_mm"); mhi = sem("mhi"); maxt_cp = sem("maxt_cp")
        adjt_mm = sem("adjt_mm"); adjt_cp = sem("adjt_cp")
        dent_mm = sem("dent_mm"); rcp_done = sem("rcp_done"); rcp_one = sem("rcp_one")
        rden_mm = sem("rden_mm"); attn_done = sem("attn_done")
        proj_mm = sem("proj_mm"); y_done = sem("y_done")
        xb_done = sem("xb_done")
        st_done = sem("st_done"); mv_one = sem("mv_one"); mv_two = sem("mv_two"); var_done = sem("var_done")
        rstd_done = sem("rstd_done"); nmean_done = sem("nmean_done"); ln_done = sem("ln_done")

        x_rows = x.rearrange("b n d -> (b n) d")
        adj_rows = adj.rearrange("b q k -> (b q) k")
        out_rows = out.rearrange("b n d -> (b n) d")
        NCH = B * NC

        block = ctx.enter_context(nc.Block())

        def batches(engine, body):
            with engine.Fori(0, B - 1) as b:
                body(b, False)
            body(B - 1, True)

        def chunk_rows(n):
            return bass.ds(n * QC, QC)

        def adj_slice(c, kt, heads):
            return adjT[:, c % 2, kt, :].unsqueeze(1).to_broadcast([P, heads, QC])

        def consumed(item, b):
            kind, k = item[0], item[1]
            if kind == "max":
                return max_red, (NPASS * b + k) * MAXP + item[2] + 1
            if kind == "max_t":
                return maxt_cp, NPASS * b + k + 1
            if kind == "adj_t":
                return adjt_cp, (NC * b + k) * KT + item[2] + 1
            if kind == "den_t":
                return rcp_done, NPASS * b + k + 1
            if kind == "rden":
                return attn_done, LEAD + NPASS * b + k + 1
            return y_done, LEAD + (NC * b + k) * QT + item[2] + 1

        @block.sync
        def _(sp):
            for done in (*hi_stored, *lo_stored, *v_stored, out_done):
                sp.sem_inc(done, LEAD)
            for w, src in enumerate((wq, wk, wv, wo)):
                sp.dma_start(w_in[:, w], src.rearrange("(o p) d -> p o d", p=P)).then_inc(w_ready, 16)
            sp.dma_start(bo_b[:, :], bo.rearrange("(a d) -> a d", a=1).to_broadcast([P, D])).then_inc(bo_ready, 16)

            def load_x(n, s):
                sp.dma_start(x_in[:, s], x_rows[chunk_rows(n), :].rearrange("(t p) d -> p t d", p=P)
                             ).then_inc(x_ready[s], 16)

            def load_k(dst, b, g, ready):
                for row, part in ((0, KHI), (1, KHI), (2, KLO)):
                    src = parts[part, bass.ds(b * D + g * P, P), :].rearrange("(h d) t -> d h t", d=HD)
                    sp.dma_start(dst[row * HD:(row + 1) * HD], src).then_inc(ready, 16)

            def load_q(b, j):
                c, g = (j % NPASS) // HG, j % HG
                row0 = b * D + (j // NPASS * D + g * P)
                for row, part in ((0, QHI), (1, QLO), (2, QHI)):
                    src = parts[part, bass.ds(row0, P), c * QC:(c + 1) * QC]
                    sp.dma_start(qst[row * HD:(row + 1) * HD, j % QRING], src.rearrange("(h d) t -> d h t", d=HD)
                                 ).then_inc(q_ready[j % QRING], 16)

            def load_v(b, g):
                src = v_rows[bass.ds(b * N, N), g * P:(g + 1) * P]
                sp.dma_start(vmain[:, g], src.rearrange("(k p) f -> p k f", p=P)).then_inc(v_ready[g], 16)

            def load_adj(c, piece):
                src = adj_rows[chunk_rows(c), piece * 2 * P:(piece + 1) * 2 * P]
                sp.dma_start(adj_nat[:, piece % 2], src.rearrange("(t p) k -> p t k", p=P)
                             ).then_inc(adj_in[piece % 2], 16)

            def place_maxima(b, j):
                sp.wait_ge(maxt_cp, NPASS * b + j + 1)
                for r in range(2):
                    sp.dma_start(qst[KROWS + r:KROWS + r + 1, j % QRING], mrow[:, r, :]
                                 ).then_inc(mrow_in[j % 2], 16)

            def store(b, c):
                sp.wait_ge(ln_done, LEAD + NC * b + c + 1)
                sp.dma_start(out_rows[chunk_rows(NC * b + c), :].rearrange("(t p) d -> p t d", p=P), y[:, :, :]
                             ).then_inc(out_done, 16)

            load_x(0, 0)
            load_x(1, 1)

            def project_batch(b, last):
                if last:
                    for s in range(2):
                        sp.wait_ge(hi_stored[s], LEAD + 32 * NC // 2)
                        sp.wait_ge(lo_stored[s], LEAD + 32 * NC // 2)
                        sp.wait_ge(v_stored[s], LEAD + 16 * NC // 2)
                    load_k(kext, 0, 0, kext_ready)
                    for j in range(QRING - 1):
                        load_q(0, j)
                    load_adj(0, 0)
                    load_adj(0, 1)
                    load_k(kmain[:, 0], 0, 0, k_ready[0])
                    load_v(0, 0)
                for c in range(NC):
                    n, s = b * NC + c, c % 2
                    if not (last and c >= NC - 2):
                        sp.wait_ge(xT_ps, DT * (n + 1))
                        load_x(n + 2, s)
                    sp.wait_ge(lo_done, LEAD + 4 * (n + 1))
                    for which, st, stored in ((0, hi_st, hi_stored), (1, lo_st, lo_stored)):
                        for w in range(2):
                            dst = parts[2 * w + which, bass.ds(b * D, D), c * QC:(c + 1) * QC]
                            sp.dma_start(dst.rearrange("(m p) q -> p m q", p=P), st[:, s, 2 * w:2 * w + 2]
                                         ).then_inc(stored[s], 16)
                    sp.wait_ge(v_done, LEAD + n + 1)
                    sp.dma_start(v_rows[chunk_rows(n), :].rearrange("(t p) d -> p t d", p=P), v_st[:, s]
                                 ).then_inc(v_stored[s], 16)

            batches(sp, project_batch)
            for s in range(2):
                sp.wait_ge(hi_stored[s], LEAD + 32 * B * NC // 2)
                sp.wait_ge(lo_stored[s], LEAD + 32 * B * NC // 2)
                sp.wait_ge(v_stored[s], LEAD + 16 * B * NC // 2)

            for piece in range(2, KT // 2 + 1):
                sp.wait_ge(adjt_mm, 2 * piece - 2)
                load_adj(piece // (KT // 2), piece % (KT // 2))
            place_maxima(0, 0)
            sp.wait_ge(max_mm, MAXP)
            load_k(kext, 0, 1, kext_ready)

            def attend_batch(b, last):
                U0 = NU * b
                for j in range(NPASS):
                    c, g = divmod(j, HG)
                    for u in range(KT):
                        step = g * KT + u
                        if j == 0 and u == 0:
                            sp.wait_ge(pv_done, U0 + RING)
                            load_k(kmain[:, 1], b, 1, k_ready[1])
                            load_v(b, 1)
                        if j == 1 and u == 0 and not last:
                            sp.wait_ge(max_mm, (NPASS * b + 2) * MAXP)
                            load_k(kext, b + 1, 0, kext_ready)
                        if j == NPASS - 1 and u == 0 and not last:
                            sp.wait_ge(pv_done, U0 + j * KT + RING)
                            load_k(kmain[:, 0], b + 1, 0, k_ready[0])
                            load_v(b + 1, 0)
                        if u == 0 and not (last and j + QRING - 1 >= NPASS):
                            sp.wait_ge(pv_done, U0 + j * KT + RING)
                            load_q(b, j + QRING - 1)
                        if g == 1 and u == 0:
                            sp.wait_ge(out_done, LEAD + 16 * (NC * b + c))
                            sp.dma_start(y[:, :, :], x_rows[chunk_rows(NC * b + c), :]
                                         .rearrange("(t p) d -> p t d", p=P)).then_inc(xres_in, 16)
                        if step % 4 == 0:
                            piece = step // 4 + 1
                            cc, k = c + 1 + piece // (KT // 2), piece % (KT // 2)
                            if not (last and cc >= NC):
                                sp.wait_ge(adjt_mm, (NC * b + cc) * KT + 2 * k - 2)
                                load_adj(NC * b + cc, k)
                        if u == MAX_AT and not (last and j == NPASS - 1):
                            place_maxima(b, j + 1)
                            if j == NPASS - 1:
                                sp.wait_ge(max_mm, (NPASS * (b + 1) + 1) * MAXP)
                                load_k(kext, b + 1, 1, kext_ready)
                        if g == 0 and j >= 2 and u == 13:
                            store(b, c - 1)
                store(b, NC - 1)

            batches(sp, attend_batch)
            sp.wait_ge(out_done, LEAD + 16 * B * NC)

        @block.tensor
        def _(pe):
            for done in (v_ps, maxt_mm):
                pe.sem_inc(done, LEAD)
            pe.wait_ge(const_ready, 4)
            pe.wait_ge(w_ready, 64)
            for w in range(4):
                for k in range(DT):
                    for o in range(DT):
                        mm = nc.tensor.transpose(ps[:, w, k * D + o * P:k * D + (o + 1) * P],
                                                 w_in[:, w, o, k * P:(k + 1) * P], ident[:, :])
                mm.then_inc(wT_ps, 1)
            pe.wait_ge(wT_done, 4)

            def project_batch(b, last):
                for c in range(NC):
                    n, s = b * NC + c, c % 2
                    pe.wait_ge(x_ready[s], 16 * (b * (NC // 2) + c // 2 + 1))
                    pe.wait_ge(xT_done, LEAD + DT * n)
                    for k in range(DT):
                        for t in range(QT):
                            mm = nc.tensor.transpose(ps[:, k, t * P:(t + 1) * P],
                                                     x_in[:, s, t, k * P:(k + 1) * P], ident[:, :])
                        mm.then_inc(xT_ps, 1)
                    pe.wait_ge(xT_done, LEAD + DT * (n + 1))
                    pe.wait_ge(lo_done, LEAD + 4 * n)
                    for f in range(4):
                        for k in range(DT):
                            mm = nc.tensor.matmul(ps[:, 2 + f, :], wT[:, f // 2, k, (f % 2) * P:(f % 2 + 1) * P],
                                                  xT[:, s, k, :], start=(k == 0), stop=(k == DT - 1))
                        mm.then_inc(qk_ps, 1)
                    pe.wait_ge(v_done, LEAD + n)
                    for t in range(QT):
                        for k in range(DT):
                            mm = nc.tensor.matmul(ps[:, 6 + t // 2, (t % 2) * D:(t % 2 + 1) * D],
                                                  xT[:, s, k, t * P:(t + 1) * P], wT[:, 2, k, :],
                                                  start=(k == 0), stop=(k == DT - 1))
                    mm.then_inc(v_ps, 1)

            batches(pe, project_batch)
            pe.wait_ge(xT_done, LEAD + DT * B * NC)
            pe.wait_ge(lo_done, LEAD + 4 * B * NC)
            pe.wait_ge(v_done, LEAD + B * NC)

            def aux_item(item, n, b):
                kind, k = item[0], item[1]
                bank = aux(n)
                if kind == "max":
                    p = item[2]
                    h, t, kc = p // (QT * 4), p // 4 % QT, p % 4
                    kst = kext if k in (0, 1, NPASS) else kmain[:, k % HG]
                    if p == 0:
                        pe.wait_ge(q_ready[k % QRING], 48 * (NPASS // QRING * b + k // QRING + 1))
                        if k in (0, 1, NPASS):
                            pe.wait_ge(kext_ready, 48 * (2 * b + (2 if k == NPASS else k) + 1))
                        else:
                            pe.wait_ge(k_ready[k % HG], 48 * (b + 1))
                    nc.tensor.matmul(bank, qst[0:KROWS, k % QRING, h, t * P:(t + 1) * P],
                                     kst[0:KROWS, h, kc * 512:(kc + 1) * 512],
                                     start=True, stop=True).then_inc(max_mm, 1)
                elif kind == "max_t":
                    pe.wait_ge(m_ready, NPASS * b + k + 1)
                    nc.tensor.transpose(bank[0:4 * QT, 0:P], m16[:, :], ident[:, :]).then_inc(maxt_mm, 1)
                elif kind == "adj_t":
                    kt = item[2]
                    if kt % 2 == 0:
                        pe.wait_ge(adj_in[kt // 2 % 2], 16 * ((NC * b + k) * (KT // 4) + kt // 4 + 1))
                    for t in range(QT):
                        mm = nc.tensor.transpose(bank[:, t * P:(t + 1) * P],
                                                 adj_nat[:, kt // 2 % 2, t, (kt % 2) * P:(kt % 2 + 1) * P],
                                                 ident[:, :])
                    mm.then_inc(adjt_mm, 1)
                elif kind == "den_t":
                    pe.wait_ge(evac, LEAD + NPASS * b + k + 1)
                    for t in range(QT):
                        mm = nc.tensor.transpose(bank[:, t * P:(t + 1) * P], den_s[:, t * P:(t + 1) * P],
                                                 ident[:, :])
                    mm.then_inc(dent_mm, 1)
                elif kind == "rden":
                    pe.wait_ge(rcp_done, NPASS * b + k + 1)
                    for t in range(QT):
                        mm = nc.tensor.matmul(bank[:, t * P:(t + 1) * P],
                                              rcp32[:, t].rearrange("p h r -> p (h r)"),
                                              ident[:, :], start=True, stop=True)
                    mm.then_inc(rden_mm, 1)
                else:
                    t = item[2]
                    if t == 0:
                        pe.wait_ge(attn_done, LEAD + HG * (NC * b + k + 1))
                    for g in range(HG):
                        mm = nc.tensor.matmul(bank[:, 0:D], attnT[:, g, t * P:(t + 1) * P], wT[:, 3, g, :],
                                              start=(g == 0), stop=(g == HG - 1))
                    mm.then_inc(proj_mm, 1)

            def aux_run(items, n, done, b):
                for item in items:
                    if n >= 2:
                        s, value = consumed(done[n - 2], b)
                        pe.wait_ge(s, value)
                    aux_item(item, n, b)
                    done.append(item)
                    n += 1
                return n

            def scores(b, j, u, a):
                g = j % HG
                if u == 0 and not a:
                    pe.wait_ge(mrow_in[j % 2], 32 * (NPASS // 2 * b + j // 2 + 1))
                    if j in (0, 1, NPASS):
                        pe.wait_ge(k_ready[g], 48 * (b + 1 + j // NPASS))
                for i in range(HA if a else 4 - HA):
                    h = i if a else HA + i
                    mm = nc.tensor.matmul((sc_a if a else sc_b)[:, i, :], kmain[:, g, h, u * P:(u + 1) * P],
                                          qst[:, j % QRING, h, :], start=True, stop=True)
                mm.then_inc(st_a if a else st_b, 1)

            aux_run(prologue_items(), 0, [], 0)
            scores(0, 0, 0, False)
            scores(0, 0, 0, True)
            pe.wait_ge(exp_b, 1)
            scores(0, 0, 1, False)
            pe.wait_ge(mul_a, LEAD + 1)
            scores(0, 0, 1, True)

            def attend_batch(b, last):
                pe.wait_ge(max_red, MAXP * (NPASS * b + 1))
                pe.wait_ge(maxt_cp, NPASS * b + 1)
                pe.wait_ge(adjt_cp, KT * (NC * b + 1))
                pe.wait_ge(y_done, LEAD + QT * NC * b)
                n, done = 0, []
                for j in range(NPASS):
                    g = j % HG
                    for u in range(KT):
                        U = NU * b + KT * j + u
                        ahead = divmod(KT * j + u + LOOK, KT)
                        more = not (last and ahead[0] == NPASS)
                        if more:
                            pe.wait_ge(exp_b, U + LOOK)
                            scores(b, *ahead, False)
                        items = aux_items(j, u, last)
                        cuts = [len(items) * i // 4 for i in range(5)]
                        if u == 0:
                            cuts[1] = cuts[2]
                        n = aux_run(items[cuts[0]:cuts[1]], n, done, b)
                        if u == 0:
                            if more:
                                pe.wait_ge(mul_a, LEAD + U + LOOK)
                                scores(b, *ahead, True)
                            pe.wait_ge(evac, LEAD + NPASS * b + j)
                            if j < HG:
                                pe.wait_ge(v_ready[g], 16 * (b + 1))
                        pe.wait_ge(mul_a, LEAD + U + 1)
                        pe.wait_ge(mul_b, LEAD + U + 1)
                        for h in range(4):
                            w = pa[:, u % RING, h, :] if h < HA else pb[:, u % RING, h - HA, :]
                            nc.tensor.matmul(pv_ps[h * HD:(h + 1) * HD, :], vmain[:, g, u, h * HD:(h + 1) * HD],
                                             w, start=(u == 0), stop=(u == KT - 1))
                        n = aux_run(items[cuts[1]:cuts[2]], n, done, b)
                        if u > 0 and more:
                            pe.wait_ge(mul_a, LEAD + U + LOOK)
                            scores(b, *ahead, True)
                        n = aux_run(items[cuts[2]:cuts[3]], n, done, b)
                        for h in range(4):
                            w = pa[:, u % RING, h, :] if h < HA else pb[:, u % RING, h - HA, :]
                            mm = nc.tensor.matmul(den_ps[h * HD:(h + 1) * HD, :], ones_v[:, :], w,
                                                  start=(u == 0), stop=(u == KT - 1))
                        mm.then_inc(pv_done, 1)
                        n = aux_run(items[cuts[3]:cuts[4]], n, done, b)
                n = aux_run(tail_items(), n, done, b)

            batches(pe, attend_batch)

        @block.scalar
        def _(act):
            for done in (xT_done, evac, ln_done):
                act.sem_inc(done, LEAD)
            for w in range(4):
                act.wait_ge(wT_ps, w + 1)
                nc.scalar.activation(wT[:, w].rearrange("p k d -> p (k d)"), ps[:, w, :], ACT.Copy
                                     ).then_inc(wT_done, 1)

            def project_batch(b, last):
                for c in range(NC):
                    n, s = b * NC + c, c % 2
                    for k in range(DT):
                        act.wait_ge(xT_ps, DT * n + k + 1)
                        if k == 0:
                            act.wait_ge(v_ps, LEAD + n)
                        nc.scalar.activation(xT[:, s, k, :], ps[:, k, :], ACT.Copy).then_inc(xT_done, 1)
                    act.wait_ge(hi_stored[s], LEAD + 32 * (b * (NC // 2) + c // 2))
                    for f in range(4):
                        act.wait_ge(qk_ps, 4 * n + f + 1)
                        nc.scalar.activation(hi_st[:, s, f, :], ps[:, 2 + f, :], ACT.Copy).then_inc(hi_done, 1)

            batches(act, project_batch)
            act.wait_ge(v_ps, LEAD + B * NC)
            for s in range(2):
                act.wait_ge(hi_stored[s], LEAD + 32 * B * NC // 2)
                act.wait_ge(lo_stored[s], LEAD + 32 * B * NC // 2)
                act.wait_ge(v_stored[s], LEAD + 16 * B * NC // 2)

            def adjacency_out(item, n, b):
                cc, kt = item[1], item[2]
                if kt == 0 and cc > 0:
                    act.wait_ge(mul_a, LEAD + NU * b + HG * KT * (cc - 1))
                    act.wait_ge(mul_b, LEAD + NU * b + HG * KT * (cc - 1))
                act.wait_ge(adjt_mm, (NC * b + cc) * KT + kt + 1)
                nc.scalar.activation(adjT[:, cc % 2, kt, :], aux(n), ACT.Copy, bias=ADJ_EPS).then_inc(adjt_cp, 1)

            def exps(b, j, u):
                U = NU * b + KT * j + u
                act.wait_ge(st_b, U + 1)
                act.wait_ge(pv_done, U + 1)
                nc.scalar.activation(pb[:, u % RING], sc_b, ACT.Exp, scale=SCALE).then_inc(exp_b, 1)
                act.wait_ge(st_a, U + 1)
                nc.scalar.activation(sc_a, sc_a, ACT.Exp, scale=SCALE).then_inc(exp_a, 1)

            def normalize(b, c):
                act.wait_ge(nmean_done, LEAD + NC * b + c + 1)
                for t in range(QT):
                    last = nc.scalar.activation(y[:, t, :], y[:, t, :], ACT.Identity,
                                                scale=rstd[:, t:t + 1], bias=nmean[:, t:t + 1])
                last.then_inc(ln_done, 1)

            for n, item in enumerate(prologue_items()):
                if item[0] == "adj_t":
                    adjacency_out(item, n, 0)
            for u in range(LOOK):
                exps(0, 0, u)

            def attend_batch(b, last):
                n = 0
                for j in range(NPASS):
                    c, g = divmod(j, HG)
                    for u in range(KT):
                        U = NU * b + KT * j + u
                        ahead = divmod(KT * j + u + LOOK, KT)
                        if not (last and ahead[0] == NPASS):
                            exps(b, *ahead)
                        for item in aux_items(j, u, last):
                            if item[0] == "adj_t":
                                adjacency_out(item, n, b)
                            n += 1
                        if g == 0 and j >= 2 and u == 12:
                            normalize(b, c - 1)
                        if u == KT - 1:
                            act.wait_ge(pv_done, U + 1 + RING)
                            act.wait_ge(attn_done, LEAD + NPASS * b + j)
                            act.wait_ge(y_done, LEAD + QT * (NC * b + c))
                            nc.scalar.activation(den_s[:, :], den_ps, ACT.Copy)
                            nc.scalar.activation(attnT[:, g, :], pv_ps, ACT.Copy).then_inc(evac, 1)
                normalize(b, NC - 1)

            batches(act, attend_batch)

        @block.vector
        def _(dve):
            for done in (lo_done, v_done, mul_a, y_done, attn_done):
                dve.sem_inc(done, LEAD)
            nc.vector.memset(kmain[KROWS:SROWS], 1.0).then_inc(const_ready, 1)

            def project_batch(b, last):
                for c in range(NC):
                    n, s = b * NC + c, c % 2
                    stored = b * (NC // 2) + c // 2
                    dve.wait_ge(lo_stored[s], LEAD + 32 * stored)
                    for f in range(4):
                        dve.wait_ge(hi_done, 4 * n + f + 1)
                        nc.vector.tensor_tensor(lo_st[:, s, f, :], ps[:, 2 + f, :], hi_st[:, s, f, :],
                                                ALU.subtract).then_inc(lo_done, 1)
                    dve.wait_ge(v_stored[s], LEAD + 16 * stored)
                    dve.wait_ge(v_ps, LEAD + n + 1)
                    nc.vector.tensor_copy(v_st[:, s].rearrange("p t d -> p (t d)"),
                                          ps[:, 6:8, :].rearrange("p a q -> p (a q)")).then_inc(v_done, 1)

            batches(dve, project_batch)

            def weights_a(b, j, u):
                U = NU * b + KT * j + u
                c, g = divmod(j, HG)
                if g == 0:
                    dve.wait_ge(adjt_cp, (NC * b + c) * KT + u + 1)
                dve.wait_ge(pv_done, U + 1)
                dve.wait_ge(exp_a, U + 1)
                nc.vector.tensor_tensor(pa[:, u % RING], sc_a, adj_slice(c, u, HA), ALU.mult).then_inc(mul_a, 1)

            def aux_out(item, n, b):
                kind, k = item[0], item[1]
                bank = aux(n)
                J = NPASS * b + k
                C = NC * b + k
                if kind == "max":
                    p = item[2]
                    dve.wait_ge(max_mm, J * MAXP + p + 1)
                    nc.vector.tensor_reduce(mpart[:, k % 2, p:p + 1], bank, AX_X, ALU.max).then_inc(max_red, 1)
                    if p == MAXP - 1:
                        dve.wait_ge(max_red, (J + 1) * MAXP)
                        dve.wait_ge(maxt_mm, LEAD + J)
                        nc.vector.tensor_reduce(m16[:, :], mpart[:, k % 2].rearrange("p (r k) -> p r k", k=4),
                                                AX_X, ALU.max).then_inc(m_ready, 1)
                elif kind == "max_t":
                    dve.wait_ge(maxt_mm, LEAD + J + 1)
                    if not isinstance(b, int) or b > 0 or k > 0:
                        dve.wait_ge(mrow_in[(k - 1) % 2], 32 * (NPASS // 2 * b + (k - 1) // 2 + 1))
                    nc.vector.tensor_scalar(mrow[:, 0, :], bank[0:4 * QT, 0:P], -1.0, None, ALU.mult
                                            ).then_inc(mhi, 1)
                    dve.wait_ge(mhi, J + 1)
                    nc.vector.scalar_tensor_tensor(mrow[:, 1, :], bank[0:4 * QT, 0:P], -1.0, mrow[:, 0, :],
                                                   ALU.mult, ALU.subtract).then_inc(maxt_cp, 1)
                elif kind == "den_t":
                    dve.wait_ge(dent_mm, J + 1)
                    nc.vector.reciprocal(rcp[:, :, :], bank.rearrange("p (t h r) -> p t h r", t=QT, h=4)[:, :, :, 0]
                                         ).then_inc(rcp_one, 1)
                    dve.wait_ge(rcp_one, J + 1)
                    nc.vector.tensor_copy(rcp32[:, :, :, :], rcp[:, :, :].unsqueeze(3).to_broadcast([P, QT, 4, HD])
                                          ).then_inc(rcp_done, 1)
                elif kind == "rden":
                    dve.wait_ge(rden_mm, J + 1)
                    nc.vector.tensor_tensor(attnT[:, k % HG, :], bank, attnT[:, k % HG, :], ALU.mult
                                            ).then_inc(attn_done, 1)
                elif kind == "proj":
                    t = item[2]
                    if t == 0:
                        dve.wait_ge(xb_done, C + 1)
                    dve.wait_ge(proj_mm, QT * C + t + 1)
                    nc.vector.tensor_tensor(y[:, t, :], bank[:, 0:D], y[:, t, :], ALU.add).then_inc(y_done, 1)
                    dve.wait_ge(y_done, LEAD + QT * C + t + 1)
                    nc.vector.bn_stats(stats[:, t, :], y[:, t, :]).then_inc(st_done, 1)
                    if t == QT - 1:
                        dve.wait_ge(st_done, QT * (C + 1))
                        dve.wait_ge(nmean_done, LEAD + C)
                        nc.vector.tensor_tensor(mv[:, 0, :], stats[:, :, 1], stats[:, :, 4], ALU.subtract)
                        nc.vector.tensor_tensor(mv[:, 1, :], stats[:, :, 1], stats[:, :, 4], ALU.add)
                        nc.vector.tensor_tensor(mv[:, 2, :], stats[:, :, 2], stats[:, :, 5], ALU.add
                                                ).then_inc(mv_one, 1)
                        dve.wait_ge(mv_one, C + 1)
                        nc.vector.scalar_tensor_tensor(mv[:, 3, :], mv[:, 0, :], 0.25, mv[:, 0, :], ALU.mult, ALU.mult)
                        nc.vector.tensor_scalar(mv[:, 4, :], mv[:, 1, :], -0.5, None, ALU.mult)
                        nc.vector.tensor_scalar(mv[:, 5, :], mv[:, 2, :], 1.0 / D, LN_EPS, ALU.mult, ALU.add
                                                ).then_inc(mv_two, 1)
                        dve.wait_ge(mv_two, C + 1)
                        nc.vector.tensor_tensor(mv[:, 6, :], mv[:, 3, :], mv[:, 5, :], ALU.add).then_inc(var_done, 1)

            for n, item in enumerate(prologue_items()):
                aux_out(item, n, 0)
            for u in range(LOOK):
                weights_a(0, 0, u)

            def attend_batch(b, last):
                n = 0
                for j in range(NPASS):
                    for u in range(KT):
                        ahead = divmod(KT * j + u + LOOK, KT)
                        for item in aux_items(j, u, last):
                            aux_out(item, n, b)
                            n += 1
                        if not (last and ahead[0] == NPASS):
                            weights_a(b, *ahead)
                for item in tail_items():
                    aux_out(item, n, b)
                    n += 1

            batches(dve, attend_batch)

        @block.gpsimd
        def _(pool):
            for done in (mul_b, nmean_done):
                pool.sem_inc(done, LEAD)
            nc.gpsimd.memset(ident[:, :], 0.0).then_inc(ident_zero, 1)
            nc.gpsimd.memset(ones_v[:, :], 1.0).then_inc(const_ready, 1)
            nc.gpsimd.memset(minus_half[:, :], -0.5).then_inc(const_ready, 1)
            pool.wait_ge(ident_zero, 1)
            nc.gpsimd.affine_select(out=ident[:, :], in_=ident[:, :], compare_op=ALU.not_equal, fill=1.0,
                                    base=0, pattern=[[-1, P]], channel_multiplier=1).then_inc(const_ready, 1)
            pool.wait_ge(bo_ready, 16)
            pool.wait_ge(const_ready, 4)

            def weights_b(b, j, u):
                U = NU * b + KT * j + u
                c, g = divmod(j, HG)
                if g == 0:
                    pool.wait_ge(adjt_cp, (NC * b + c) * KT + u + 1)
                pool.wait_ge(exp_b, U + 1)
                nc.gpsimd.tensor_tensor(pb[:, u % RING], pb[:, u % RING], adj_slice(c, u, 4 - HA), ALU.mult
                                        ).then_inc(mul_b, 1)

            def add_bias(b, c):
                pool.wait_ge(xres_in, 16 * (NC * b + c + 1))
                nc.gpsimd.tensor_tensor(y[:, :, :], y[:, :, :],
                                        bo_b[:, :].unsqueeze(1).to_broadcast([P, QT, D]), ALU.add
                                        ).then_inc(xb_done, 1)

            def norm_scalars(b, c):
                C = NC * b + c
                pool.wait_ge(var_done, C + 1)
                pool.wait_ge(ln_done, LEAD + C)
                nc.gpsimd.tensor_tensor(rstd[:, :], mv[:, 6, :], minus_half[:, :], ALU.pow).then_inc(rstd_done, 1)
                pool.wait_ge(rstd_done, C + 1)
                nc.gpsimd.tensor_tensor(nmean[:, :], mv[:, 4, :], rstd[:, :], ALU.mult
                                        ).then_inc(nmean_done, 1)

            pool.sem_inc(pv_done, RING)
            weights_b(0, 0, 0)

            def attend_batch(b, last):
                for j in range(NPASS):
                    c, g = divmod(j, HG)
                    for u in range(KT):
                        if not (last and j == NPASS - 1 and u == KT - 1):
                            weights_b(b, *divmod(KT * j + u + 1, KT))
                        if g == 1 and u == 8:
                            add_bias(b, c)
                        if g == 0 and j >= 2 and u == 10:
                            norm_scalars(b, c - 1)
                norm_scalars(b, NC - 1)

            batches(pool, attend_batch)


_INS = ["x", "adj", "L0_gnn_Wq", "L0_gnn_Wk", "L0_gnn_Wv", "L0_gnn_Wo", "L0_gnn_bo"]


def kernel(**inputs):
    import numpy as _np
    import concourse.bacc as _bacc
    from concourse import mybir as _mybir
    from concourse.bass_utils import run_bass_kernel_spmd as _run

    nc = _bacc.Bacc("TRN2", target_bir_lowering=False, num_devices=1)
    arrays, args = {}, []
    for name in _INS:
        a = _np.ascontiguousarray(inputs[name])
        arrays[f"in_{name}"] = a
        args.append(nc.dram_tensor(f"in_{name}", a.shape, _mybir.dt.from_np(a.dtype), kind="ExternalInput").ap())
    out = nc.dram_tensor("out", (B, N, D), F32, kind="ExternalOutput")
    attention_layer(nc, *args, out.ap())
    r = _run(nc, [arrays], core_ids=[0])
    return r.results[0]["out"]
```

```python
from contextlib import ExitStack

import concourse.bass as bass
from concourse import mybir

P = 128
F32 = mybir.dt.float32
F16 = mybir.dt.float16
ALU = mybir.AluOpType
ACT = mybir.ActivationFunctionType
AX_X = mybir.AxisListType.X

B, N, D, H = 8, 2048, 256, 8
HD = D // H
QC = 512
NC = N // QC
QT = QC // P
KT = N // P
HG = H // 4
NPASS = NC * HG
NU = NPASS * KT
DT = D // P
SCALE = float(HD) ** -0.5
ADJ_EPS = 1e-6
LN_EPS = 1e-5
X_UP, W_UP = 16.0, 64.0
DOWN = 1.0 / (X_UP * W_UP)
KROWS = 3 * HD
SROWS = KROWS + 2
RING = 4
QRING = 4
MAXP = 4 * QT * (N // 512)
MAX_AT = 12
HB = 3
AUX = 3
LEAD = 16
LOOK = 2


def aux_items(j, u, skip_next):
    c, g = divmod(j, HG)
    items = []
    if j >= 1 and u == 1:
        items.append(("den_t", j - 1))
    if j >= 1 and u == 3:
        items.append(("rden", j - 1))
    if j >= 2 and g == 0 and 5 <= u < 5 + QT:
        items.append(("proj", c - 1, u - 5))
    if j == 0 and u < MAX_AT:
        items += [("max", 1, p) for p in range(MAXP) if p * MAX_AT // MAXP == u]
    k = j + 1 if u < MAX_AT else j + 2
    if 2 <= k <= NPASS and not (skip_next and k == NPASS):
        at = (u - MAX_AT) % KT
        items += [("max", k, p) for p in range(MAXP) if p * KT // MAXP == at]
    if u == MAX_AT and not (skip_next and j == NPASS - 1):
        items.append(("max_t", j + 1))
    if u % 2 == 0 and not (skip_next and c == NC - 1):
        items.append(("adj_t", c + 1, g * (KT // 2) + u // 2))
    return items


STEP = "b0 b1 0 pv b2 1 a 2 den 3"
FIRST_STEP = "b0 0 b1 1 a 2 pv b2 den 3"


def step(j, u, skip_next):
    items = aux_items(j, u, skip_next)
    ahead = not (skip_next and KT * j + u + LOOK >= NU)
    cut = [len(items) * i // 4 for i in range(5)]
    order = []
    for word in (FIRST_STEP if u == 0 else STEP).split():
        if word.isdigit():
            order += items[cut[int(word)]:cut[int(word) + 1]]
        elif word in ("pv", "den") or ahead:
            order.append((word,))
    return order


def tail_items():
    return [("den_t", NPASS - 1), ("rden", NPASS - 1)] + [("proj", NC - 1, t) for t in range(QT)]


def prologue_items():
    items = []
    for kt in range(KT):
        items += [("max", 0, p) for p in range(kt * MAXP // KT, (kt + 1) * MAXP // KT)]
        items.append(("adj_t", 0, kt))
    return items + [("max_t", 0)]


def attention_layer(nc, x, adj, wq, wk, wv, wo, bo, out):
    ctx = ExitStack()
    with ctx:
        def sb(name, shape, dt):
            return ctx.enter_context(nc.sbuf_tensor(name, shape, dt))

        def sem(name):
            return ctx.enter_context(nc.semaphore(name))

        parts = nc.dram_tensor("qk_parts", [4, B * D, N], F16, kind="Internal").ap()
        QHI, QLO, KHI, KLO = range(4)
        v_rows = nc.dram_tensor("v_rows", [B * N, D], F32, kind="Internal").ap()

        ident = sb("ident", [P, P], F32)
        ones_v = sb("ones_v", [P, HD], F32)
        woT = sb("woT", [P, DT, D], F32)
        bo_b = sb("bo_b", [P, D], F32)
        minus_half = sb("minus_half", [P, QT], F32)
        adjT = sb("adjT", [P, 2, KT, QC], F32)
        adj_nat = sb("adj_nat", [P, 2, QT, 2 * P], F32)
        kmain = sb("kmain", [SROWS, 2, 4, N], F16)
        kext = sb("kext", [SROWS, 4, N], F16)
        vmain = sb("vmain", [P, 2, KT, P], F32)
        qst = sb("qst", [SROWS, QRING, 4, QC], F16)
        pa = sb("pa", [P, RING, QC], F32)
        pb = sb("pb", [P, RING, HB, QC], F32)
        mpart = sb("mpart", [P, 2, MAXP], F32)
        m16 = sb("m16", [P, 4 * QT], F32)
        mrow = sb("mrow", [4 * QT, 2, P], F16)
        den_s = sb("den_s", [P, QC], F32)
        rcp = sb("rcp", [P, QT, 4], F32)
        rcp32 = sb("rcp32", [P, QT, 4, HD], F32)
        attnT = sb("attnT", [P, HG, QC], F32)
        y = sb("y", [P, QT, D], F32)
        stats = sb("stats", [P, QT, 6], F32)
        mv = sb("mv", [P, 7, QT], F32)
        rstd = sb("rstd", [P, QT], F32)
        nmean = sb("nmean", [P, QT], F32)

        flat = adjT[:, :, :, :].rearrange("p a k q -> p (a k q)")
        W = QT * D
        x_in = flat[:, 0:2 * W].rearrange("p (s t d) -> p s t d", s=2, t=QT)
        xh = flat[:, 2 * W:3 * W].bitcast(F16).rearrange("p (s k q) -> p s k q", s=2, k=DT)
        xl = flat[:, 3 * W:4 * W].bitcast(F16).rearrange("p (s k q) -> p s k q", s=2, k=DT)
        v_st = flat[:, 4 * W:6 * W].rearrange("p (s t d) -> p s t d", s=2, t=QT)
        hi_st = flat[:, 6 * W:8 * W].bitcast(F16).rearrange("p (s f q) -> p s f q", s=2, f=4)
        lo_st = flat[:, 8 * W:10 * W].bitcast(F16).rearrange("p (s f q) -> p s f q", s=2, f=4)
        w_in = flat[:, 10 * W:12 * W].rearrange("p (w o d) -> p w o d", w=4, o=DT)
        wh, wl = (flat[:, at * W:at * W + 3 * DT * D // 2].bitcast(F16).rearrange("p (w k d) -> p w k d", w=3, k=DT)
                  for at in (12, 14))

        ps = ctx.enter_context(nc.psum_tensor("ps", [P, 8, 512], F32))
        sc_a = ps[:, 2, :]
        pv_ps = ps[:, 3, :]
        den_ps = ps[:, 4, :]

        def sc_b(u, i):
            return ps[:, (HB * u + i) % 2, :]

        def aux(n):
            return ps[:, 5 + n % AUX, :]

        w_ready = sem("w_ready"); bo_ready = sem("bo_ready")
        const_ready = sem("const_ready"); ident_zero = sem("ident_zero"); k_ones = sem("k_ones")
        wT_ps = sem("wT_ps"); wh_done = sem("wh_done"); wl_done = sem("wl_done")
        x_ready = [sem("x_ready0"), sem("x_ready1")]
        xT_ps = sem("xT_ps"); xh_done = sem("xh_done"); xl_done = sem("xl_done")
        qk_ps = sem("qk_ps"); hi_done = sem("hi_done"); lo_done = sem("lo_done")
        v_ps = sem("v_ps"); v_done = sem("v_done")
        hi_stored = [sem("hi_stored0"), sem("hi_stored1")]
        lo_stored = [sem("lo_stored0"), sem("lo_stored1")]
        v_stored = [sem("v_stored0"), sem("v_stored1")]

        k_ready = [sem("k_ready0"), sem("k_ready1")]; kext_ready = sem("kext_ready")
        v_ready = [sem("v_ready0"), sem("v_ready1")]
        q_ready = [sem(f"q_ready{i}") for i in range(QRING)]
        mrow_in = [sem("mrow_in0"), sem("mrow_in1")]
        adj_in = [sem("adj_in0"), sem("adj_in1")]
        xres_in = sem("xres_in"); out_done = sem("out_done")
        st_a = sem("st_a"); st_b = sem("st_b")
        exp_a = sem("exp_a"); exp_b = sem("exp_b")
        mul_a = sem("mul_a"); mul_b = sem("mul_b")
        pv_done = sem("pv_done")
        evac = sem("evac")
        max_mm = sem("max_mm"); max_red = sem("max_red")
        m_ready = sem("m_ready"); maxt_mm = sem("maxt_mm"); mhi = sem("mhi"); maxt_cp = sem("maxt_cp")
        adjt_mm = sem("adjt_mm"); adjt_cp = sem("adjt_cp")
        dent_mm = sem("dent_mm"); rcp_done = sem("rcp_done"); rcp_one = sem("rcp_one")
        rden_mm = sem("rden_mm"); attn_done = sem("attn_done")
        proj_mm = sem("proj_mm"); y_done = sem("y_done")
        xb_done = sem("xb_done")
        st_done = sem("st_done"); mv_one = sem("mv_one"); mv_two = sem("mv_two"); var_done = sem("var_done")
        rstd_done = sem("rstd_done"); nmean_done = sem("nmean_done"); ln_done = sem("ln_done")

        x_rows = x.rearrange("b n d -> (b n) d")
        adj_rows = adj.rearrange("b q k -> (b q) k")
        out_rows = out.rearrange("b n d -> (b n) d")
        NCH = B * NC

        block = ctx.enter_context(nc.Block())

        def batches(engine, body):
            with engine.Fori(0, B - 1) as b:
                body(b, False)
            body(B - 1, True)

        def chunk_rows(n):
            return bass.ds(n * QC, QC)

        def consumed(item, b):
            kind, k = item[0], item[1]
            if kind == "max":
                return max_red, (NPASS * b + k) * MAXP + item[2] + 1
            if kind == "max_t":
                return maxt_cp, NPASS * b + k + 1
            if kind == "adj_t":
                return adjt_cp, (NC * b + k) * KT + item[2] + 1
            if kind == "den_t":
                return rcp_done, NPASS * b + k + 1
            if kind == "rden":
                return attn_done, LEAD + NPASS * b + k + 1
            return y_done, LEAD + (NC * b + k) * QT + item[2] + 1

        @block.sync
        def _(sp):
            for done in (*hi_stored, *lo_stored, *v_stored, out_done):
                sp.sem_inc(done, LEAD)
            for w, src in enumerate((wq, wk, wv, wo)):
                sp.dma_start(w_in[:, w], src.rearrange("(o p) d -> p o d", p=P)).then_inc(w_ready, 16)
            sp.dma_start(bo_b[:, :], bo.rearrange("(a d) -> a d", a=1).to_broadcast([P, D])).then_inc(bo_ready, 16)

            def load_x(n, s):
                sp.dma_start(x_in[:, s], x_rows[chunk_rows(n), :].rearrange("(t p) d -> p t d", p=P)
                             ).then_inc(x_ready[s], 16)

            def load_k(dst, b, g, ready):
                for row, part in ((0, KHI), (1, KHI), (2, KLO)):
                    src = parts[part, bass.ds(b * D + g * P, P), :].rearrange("(h d) t -> d h t", d=HD)
                    sp.dma_start(dst[row * HD:(row + 1) * HD], src).then_inc(ready, 16)

            def load_q(b, j):
                c, g = (j % NPASS) // HG, j % HG
                row0 = b * D + (j // NPASS * D + g * P)
                for row, part in ((0, QHI), (1, QLO), (2, QHI)):
                    src = parts[part, bass.ds(row0, P), c * QC:(c + 1) * QC]
                    sp.dma_start(qst[row * HD:(row + 1) * HD, j % QRING], src.rearrange("(h d) t -> d h t", d=HD)
                                 ).then_inc(q_ready[j % QRING], 16)

            def load_v(b, g):
                src = v_rows[bass.ds(b * N, N), g * P:(g + 1) * P]
                sp.dma_start(vmain[:, g], src.rearrange("(k p) f -> p k f", p=P)).then_inc(v_ready[g], 16)

            def load_adj(c, piece):
                src = adj_rows[chunk_rows(c), piece * 2 * P:(piece + 1) * 2 * P]
                sp.dma_start(adj_nat[:, piece % 2], src.rearrange("(t p) k -> p t k", p=P)
                             ).then_inc(adj_in[piece % 2], 16)

            def place_maxima(b, j):
                sp.wait_ge(maxt_cp, NPASS * b + j + 1)
                for r in range(2):
                    sp.dma_start(qst[KROWS + r:KROWS + r + 1, j % QRING], mrow[:, r, :]
                                 ).then_inc(mrow_in[j % 2], 16)

            def store(b, c):
                sp.wait_ge(ln_done, LEAD + NC * b + c + 1)
                sp.dma_start(out_rows[chunk_rows(NC * b + c), :].rearrange("(t p) d -> p t d", p=P), y[:, :, :]
                             ).then_inc(out_done, 16)

            load_x(0, 0)
            load_x(1, 1)

            def project_batch(b, last):
                if last:
                    for s in range(2):
                        sp.wait_ge(hi_stored[s], LEAD + 32 * NC // 2)
                        sp.wait_ge(lo_stored[s], LEAD + 32 * NC // 2)
                        sp.wait_ge(v_stored[s], LEAD + 16 * NC // 2)
                    load_k(kext, 0, 0, kext_ready)
                    for j in range(QRING - 1):
                        load_q(0, j)
                    load_adj(0, 0)
                    load_adj(0, 1)
                    load_k(kmain[:, 0], 0, 0, k_ready[0])
                    load_v(0, 0)
                for c in range(NC):
                    n, s = b * NC + c, c % 2
                    if not (last and c >= NC - 2):
                        sp.wait_ge(xT_ps, DT * (n + 1))
                        load_x(n + 2, s)
                    sp.wait_ge(lo_done, LEAD + 4 * (n + 1))
                    for which, st, stored in ((0, hi_st, hi_stored), (1, lo_st, lo_stored)):
                        for w in range(2):
                            dst = parts[2 * w + which, bass.ds(b * D, D), c * QC:(c + 1) * QC]
                            sp.dma_start(dst.rearrange("(m p) q -> p m q", p=P), st[:, s, 2 * w:2 * w + 2]
                                         ).then_inc(stored[s], 16)
                    sp.wait_ge(v_done, LEAD + n + 1)
                    sp.dma_start(v_rows[chunk_rows(n), :].rearrange("(t p) d -> p t d", p=P), v_st[:, s]
                                 ).then_inc(v_stored[s], 16)

            batches(sp, project_batch)
            for s in range(2):
                sp.wait_ge(hi_stored[s], LEAD + 32 * B * NC // 2)
                sp.wait_ge(lo_stored[s], LEAD + 32 * B * NC // 2)
                sp.wait_ge(v_stored[s], LEAD + 16 * B * NC // 2)

            for piece in range(2, KT // 2 + 1):
                sp.wait_ge(adjt_mm, 2 * piece - 2)
                load_adj(piece // (KT // 2), piece % (KT // 2))
            place_maxima(0, 0)
            sp.wait_ge(max_mm, MAXP)
            load_k(kext, 0, 1, kext_ready)

            def attend_batch(b, last):
                U0 = NU * b
                for j in range(NPASS):
                    c, g = divmod(j, HG)
                    for u in range(KT):
                        step = g * KT + u
                        if j == 0 and u == 0:
                            sp.wait_ge(pv_done, U0 + RING)
                            load_k(kmain[:, 1], b, 1, k_ready[1])
                            load_v(b, 1)
                        if j == 1 and u == 0 and not last:
                            sp.wait_ge(max_mm, (NPASS * b + 2) * MAXP)
                            load_k(kext, b + 1, 0, kext_ready)
                        if j == NPASS - 1 and u == 0 and not last:
                            sp.wait_ge(pv_done, U0 + j * KT + RING)
                            load_k(kmain[:, 0], b + 1, 0, k_ready[0])
                            load_v(b + 1, 0)
                        if u == 0 and not (last and j + QRING - 1 >= NPASS):
                            sp.wait_ge(pv_done, U0 + j * KT + RING)
                            load_q(b, j + QRING - 1)
                        if g == 1 and u == 0:
                            if c > 0:
                                store(b, c - 1)
                            sp.wait_ge(out_done, LEAD + 16 * (NC * b + c))
                            sp.dma_start(y[:, :, :], x_rows[chunk_rows(NC * b + c), :]
                                         .rearrange("(t p) d -> p t d", p=P)).then_inc(xres_in, 16)
                        if step % 4 == 0:
                            piece = step // 4 + 1
                            cc, k = c + 1 + piece // (KT // 2), piece % (KT // 2)
                            if not (last and cc >= NC):
                                sp.wait_ge(adjt_mm, (NC * b + cc) * KT + 2 * k - 2)
                                load_adj(NC * b + cc, k)
                        if u == MAX_AT and not (last and j == NPASS - 1):
                            place_maxima(b, j + 1)
                            if j == NPASS - 1:
                                sp.wait_ge(max_mm, (NPASS * (b + 1) + 1) * MAXP)
                                load_k(kext, b + 1, 1, kext_ready)
                store(b, NC - 1)

            batches(sp, attend_batch)
            sp.wait_ge(out_done, LEAD + 16 * B * NC)

        @block.tensor
        def _(pe):
            for done in (v_ps, maxt_mm):
                pe.sem_inc(done, LEAD)
            pe.wait_ge(const_ready, 3)
            pe.wait_ge(w_ready, 64)
            for w in range(4):
                for k in range(DT):
                    for o in range(DT):
                        mm = nc.tensor.transpose(ps[:, w, k * D + o * P:k * D + (o + 1) * P],
                                                 w_in[:, w, o, k * P:(k + 1) * P], ident[:, :])
                mm.then_inc(wT_ps, 1)
            pe.wait_ge(wh_done, 4)
            pe.wait_ge(wl_done, 3)

            def transpose_x(n, s, loads):
                pe.wait_ge(x_ready[s], 16 * loads)
                for k in range(DT):
                    for t in range(QT):
                        mm = nc.tensor.transpose(ps[:, k, t * P:(t + 1) * P],
                                                 x_in[:, s, t, k * P:(k + 1) * P], ident[:, :])
                    mm.then_inc(xT_ps, 1)

            def product(out, left, right):
                pairs = ((0, 0), (0, 1), (1, 0))
                for i, (l, r) in enumerate(pairs):
                    for k in range(DT):
                        mm = nc.tensor.matmul(out, left[l][k], right[r][k], start=(i == 0 and k == 0),
                                              stop=(i == len(pairs) - 1 and k == DT - 1))
                return mm

            def project_batch(b, last):
                for c in range(NC):
                    n, s = b * NC + c, c % 2
                    x_parts = [[part[:, s, k, :] for k in range(DT)] for part in (xh, xl)]
                    pe.wait_ge(xl_done, DT * (n + 1))
                    for f in range(4):
                        pe.wait_ge(lo_done, LEAD + 4 * n - 3 + f)
                        w_parts = [[part[:, f // 2, k, (f % 2) * P:(f % 2 + 1) * P] for k in range(DT)]
                                   for part in (wh, wl)]
                        product(ps[:, 2 + f, :], w_parts, x_parts).then_inc(qk_ps, 1)
                    if not (last and c == NC - 1):
                        transpose_x(n + 1, (c + 1) % 2, b * (NC // 2) + (c + 1) // 2 + 1)
                    pe.wait_ge(v_done, LEAD + n)
                    w_parts = [[part[:, 2, k, :] for k in range(DT)] for part in (wh, wl)]
                    for t in range(QT):
                        tile = [[x[:, t * P:(t + 1) * P] for x in part] for part in x_parts]
                        mm = product(ps[:, 6 + t // 2, (t % 2) * D:(t % 2 + 1) * D], tile, w_parts)
                    mm.then_inc(v_ps, 1)

            transpose_x(0, 0, 1)
            batches(pe, project_batch)
            pe.wait_ge(xl_done, DT * B * NC)
            pe.wait_ge(lo_done, LEAD + 4 * B * NC)
            pe.wait_ge(v_done, LEAD + B * NC)
            pe.wait_ge(k_ones, 1)

            def aux_item(item, n, b):
                kind, k = item[0], item[1]
                bank = aux(n)
                if kind == "max":
                    p = item[2]
                    h, t, kc = p // (QT * 4), p // 4 % QT, p % 4
                    kst = kext if k in (0, 1, NPASS) else kmain[:, k % HG]
                    if p == 0:
                        pe.wait_ge(q_ready[k % QRING], 48 * (NPASS // QRING * b + k // QRING + 1))
                        if k in (0, 1, NPASS):
                            pe.wait_ge(kext_ready, 48 * (2 * b + (2 if k == NPASS else k) + 1))
                        else:
                            pe.wait_ge(k_ready[k % HG], 48 * (b + 1))
                    nc.tensor.matmul(bank, qst[0:KROWS, k % QRING, h, t * P:(t + 1) * P],
                                     kst[0:KROWS, h, kc * 512:(kc + 1) * 512],
                                     start=True, stop=True).then_inc(max_mm, 1)
                elif kind == "max_t":
                    pe.wait_ge(m_ready, NPASS * b + k + 1)
                    nc.tensor.transpose(bank[0:4 * QT, 0:P], m16[:, :], ident[:, :]).then_inc(maxt_mm, 1)
                elif kind == "adj_t":
                    kt = item[2]
                    if kt % 2 == 0:
                        pe.wait_ge(adj_in[kt // 2 % 2], 16 * ((NC * b + k) * (KT // 4) + kt // 4 + 1))
                    for t in range(QT):
                        mm = nc.tensor.transpose(bank[:, t * P:(t + 1) * P],
                                                 adj_nat[:, kt // 2 % 2, t, (kt % 2) * P:(kt % 2 + 1) * P],
                                                 ident[:, :])
                    mm.then_inc(adjt_mm, 1)
                elif kind == "den_t":
                    pe.wait_ge(evac, LEAD + NPASS * b + k + 1)
                    for t in range(QT):
                        mm = nc.tensor.transpose(bank[:, t * P:(t + 1) * P], den_s[:, t * P:(t + 1) * P],
                                                 ident[:, :])
                    mm.then_inc(dent_mm, 1)
                elif kind == "rden":
                    pe.wait_ge(rcp_done, NPASS * b + k + 1)
                    for t in range(QT):
                        mm = nc.tensor.transpose(bank[:, t * P:(t + 1) * P],
                                                 rcp32[:, t].rearrange("p h r -> p (h r)"), ident[:, :])
                    mm.then_inc(rden_mm, 1)
                else:
                    t = item[2]
                    if t == 0:
                        pe.wait_ge(attn_done, LEAD + HG * (NC * b + k + 1))
                    for g in range(HG):
                        mm = nc.tensor.matmul(bank[:, 0:D], attnT[:, g, t * P:(t + 1) * P], woT[:, g, :],
                                              start=(g == 0), stop=(g == HG - 1))
                    mm.then_inc(proj_mm, 1)

            def aux_run(item, done, b):
                if len(done) >= AUX:
                    s, value = consumed(done[len(done) - AUX], b)
                    pe.wait_ge(s, value)
                aux_item(item, len(done), b)
                done.append(item)

            def score(b, j, u, h):
                g = j % HG
                U = NU * b + KT * j + u
                if u == 0:
                    pe.wait_ge(mrow_in[j % 2], 32 * (NPASS // 2 * b + j // 2 + 1))
                    if j in (0, 1, NPASS):
                        pe.wait_ge(k_ready[g], 48 * (b + 1 + j // NPASS))
                if h == 0:
                    if not (isinstance(U, int) and U == 0):
                        pe.wait_ge(mul_a, LEAD + U)
                    nc.tensor.matmul(sc_a, kmain[:, g, h, u * P:(u + 1) * P], qst[:, j % QRING, h, :],
                                     start=True, stop=True).then_inc(st_a, 1)
                else:
                    i = h - 1
                    if not (isinstance(U, int) and HB * U + i < 2):
                        pe.wait_ge(exp_b, HB * U + i - 1)
                    nc.tensor.matmul(sc_b(u, i), kmain[:, g, h, u * P:(u + 1) * P], qst[:, j % QRING, h, :],
                                     start=True, stop=True).then_inc(st_b, 1)

            done = []
            for item in prologue_items():
                aux_run(item, done, 0)
            for u in range(LOOK):
                for h in (1, 2, 3, 0):
                    score(0, 0, u, h)

            def attend_batch(b, last):
                pe.wait_ge(max_red, MAXP * (NPASS * b + 1))
                pe.wait_ge(maxt_cp, NPASS * b + 1)
                pe.wait_ge(adjt_cp, KT * (NC * b + 1))
                pe.wait_ge(y_done, LEAD + QT * NC * b)
                done = []
                for j in range(NPASS):
                    g = j % HG
                    for u in range(KT):
                        U = NU * b + KT * j + u
                        ahead = divmod(KT * j + u + LOOK, KT)
                        weights = [pa[:, u % RING, :]] + [pb[:, u % RING, i, :] for i in range(HB)]
                        for what in step(j, u, last):
                            if what[0] == "a":
                                score(b, *ahead, 0)
                            elif what[0] in ("b0", "b1", "b2"):
                                score(b, *ahead, 1 + int(what[0][1]))
                            elif what[0] == "pv":
                                if u == 0:
                                    pe.wait_ge(evac, LEAD + NPASS * b + j)
                                    if j < HG:
                                        pe.wait_ge(v_ready[g], 16 * (b + 1))
                                pe.wait_ge(mul_a, LEAD + U + 1)
                                pe.wait_ge(mul_b, LEAD + U + 1)
                                for h in range(4):
                                    nc.tensor.matmul(pv_ps[h * HD:(h + 1) * HD, :],
                                                     vmain[:, g, u, h * HD:(h + 1) * HD], weights[h],
                                                     start=(u == 0), stop=(u == KT - 1))
                            elif what[0] == "den":
                                for h in range(4):
                                    mm = nc.tensor.matmul(den_ps[h * HD:(h + 1) * HD, :], ones_v[:, :], weights[h],
                                                          start=(u == 0), stop=(u == KT - 1))
                                mm.then_inc(pv_done, 1)
                            else:
                                aux_run(what, done, b)
                for item in tail_items():
                    aux_run(item, done, b)

            batches(pe, attend_batch)

        @block.scalar
        def _(act):
            for done in (evac, ln_done):
                act.sem_inc(done, LEAD)
            for w in range(4):
                act.wait_ge(wT_ps, w + 1)
                dst = (wh[:, w] if w < 3 else woT[:, :, :]).rearrange("p k d -> p (k d)")
                nc.scalar.activation(dst, ps[:, w, :], ACT.Copy, scale=W_UP if w < 3 else 1.0).then_inc(wh_done, 1)

            def x_high(n, s):
                for k in range(DT):
                    act.wait_ge(xT_ps, DT * n + k + 1)
                    if k == 0:
                        act.wait_ge(v_ps, LEAD + n - 1)
                    nc.scalar.activation(xh[:, s, k, :], ps[:, k, :], ACT.Copy, scale=X_UP).then_inc(xh_done, 1)

            def project_batch(b, last):
                for c in range(NC):
                    n, s = b * NC + c, c % 2
                    act.wait_ge(hi_stored[s], LEAD + 32 * (b * (NC // 2) + c // 2))
                    for f in range(4):
                        act.wait_ge(qk_ps, 4 * n + f + 1)
                        nc.scalar.activation(hi_st[:, s, f, :], ps[:, 2 + f, :], ACT.Copy, scale=DOWN
                                             ).then_inc(hi_done, 1)
                    if not (last and c == NC - 1):
                        x_high(n + 1, (c + 1) % 2)

            x_high(0, 0)
            batches(act, project_batch)
            act.wait_ge(v_ps, LEAD + B * NC)
            for s in range(2):
                act.wait_ge(hi_stored[s], LEAD + 32 * B * NC // 2)
                act.wait_ge(lo_stored[s], LEAD + 32 * B * NC // 2)
                act.wait_ge(v_stored[s], LEAD + 16 * B * NC // 2)

            def adjacency_out(item, n, b):
                cc, kt = item[1], item[2]
                if kt == 0 and cc > 0:
                    act.wait_ge(mul_a, LEAD + NU * b + HG * KT * (cc - 1))
                    act.wait_ge(mul_b, LEAD + NU * b + HG * KT * (cc - 1))
                act.wait_ge(adjt_mm, (NC * b + cc) * KT + kt + 1)
                nc.scalar.activation(adjT[:, cc % 2, kt, :], aux(n), ACT.Copy, bias=ADJ_EPS).then_inc(adjt_cp, 1)

            def exp_b_head(b, j, u, i):
                U = NU * b + KT * j + u
                if i == 0:
                    act.wait_ge(pv_done, U + 1)
                act.wait_ge(st_b, HB * U + i + 1)
                nc.scalar.activation(pb[:, u % RING, i, :], sc_b(u, i), ACT.Exp, scale=SCALE).then_inc(exp_b, 1)

            def exp_a_head(b, j, u):
                act.wait_ge(st_a, NU * b + KT * j + u + 1)
                nc.scalar.activation(sc_a, sc_a, ACT.Exp, scale=SCALE).then_inc(exp_a, 1)

            def normalize(b, c, t):
                if t == 0:
                    act.wait_ge(nmean_done, LEAD + NC * b + c + 1)
                norm = nc.scalar.activation(y[:, t, :], y[:, t, :], ACT.Identity,
                                            scale=rstd[:, t:t + 1], bias=nmean[:, t:t + 1])
                if t == QT - 1:
                    norm.then_inc(ln_done, 1)

            for n, item in enumerate(prologue_items()):
                if item[0] == "adj_t":
                    adjacency_out(item, n, 0)
            for u in range(LOOK):
                for i in range(HB):
                    exp_b_head(0, 0, u, i)
                exp_a_head(0, 0, u)

            def attend_batch(b, last):
                n = 0
                for j in range(NPASS):
                    c, g = divmod(j, HG)
                    for u in range(KT):
                        U = NU * b + KT * j + u
                        ahead = divmod(KT * j + u + LOOK, KT)
                        for what in step(j, u, last):
                            if what[0] == "a":
                                exp_a_head(b, *ahead)
                            elif what[0] in ("b0", "b1", "b2"):
                                exp_b_head(b, *ahead, int(what[0][1]))
                            elif what[0] not in ("pv", "den"):
                                if what[0] == "adj_t":
                                    adjacency_out(what, n, b)
                                n += 1
                        if g == 0 and j >= 2 and u >= KT - QT:
                            normalize(b, c - 1, u - (KT - QT))
                        if u == KT - 1:
                            act.wait_ge(pv_done, U + 1 + RING)
                            act.wait_ge(attn_done, LEAD + NPASS * b + j)
                            act.wait_ge(y_done, LEAD + QT * (NC * b + c))
                            nc.scalar.activation(den_s[:, :], den_ps, ACT.Copy)
                            nc.scalar.activation(attnT[:, g, :], pv_ps, ACT.Copy).then_inc(evac, 1)
                for t in range(QT):
                    normalize(b, NC - 1, t)

            batches(act, attend_batch)

        @block.vector
        def _(dve):
            for done in (lo_done, v_done, mul_a, y_done, attn_done):
                dve.sem_inc(done, LEAD)
            for w in range(3):
                dve.wait_ge(wh_done, w + 1)
                nc.vector.scalar_tensor_tensor(wl[:, w].rearrange("p k d -> p (k d)"), ps[:, w, :], W_UP,
                                               wh[:, w].rearrange("p k d -> p (k d)"), ALU.mult, ALU.subtract
                                               ).then_inc(wl_done, 1)

            def x_low(n, s):
                dve.wait_ge(v_ps, LEAD + n - 1)
                for k in range(DT):
                    dve.wait_ge(xh_done, DT * n + k + 1)
                    nc.vector.scalar_tensor_tensor(xl[:, s, k, :], ps[:, k, :], X_UP, xh[:, s, k, :],
                                                   ALU.mult, ALU.subtract).then_inc(xl_done, 1)

            def project_batch(b, last):
                for c in range(NC):
                    n, s = b * NC + c, c % 2
                    stored = b * (NC // 2) + c // 2
                    dve.wait_ge(lo_stored[s], LEAD + 32 * stored)
                    for f in range(4):
                        dve.wait_ge(hi_done, 4 * n + f + 1)
                        nc.vector.scalar_tensor_tensor(lo_st[:, s, f, :], ps[:, 2 + f, :], DOWN, hi_st[:, s, f, :],
                                                       ALU.mult, ALU.subtract).then_inc(lo_done, 1)
                    if not (last and c == NC - 1):
                        x_low(n + 1, (c + 1) % 2)
                    dve.wait_ge(v_stored[s], LEAD + 16 * stored)
                    dve.wait_ge(v_ps, LEAD + n + 1)
                    nc.vector.tensor_scalar(v_st[:, s].rearrange("p t d -> p (t d)"),
                                            ps[:, 6:8, :].rearrange("p a q -> p (a q)"), DOWN, None, ALU.mult
                                            ).then_inc(v_done, 1)

            x_low(0, 0)
            batches(dve, project_batch)

            def weights_a(b, j, u):
                U = NU * b + KT * j + u
                c, g = divmod(j, HG)
                if g == 0:
                    dve.wait_ge(adjt_cp, (NC * b + c) * KT + u + 1)
                dve.wait_ge(pv_done, U + 1)
                dve.wait_ge(exp_a, U + 1)
                nc.vector.tensor_tensor(pa[:, u % RING], sc_a, adjT[:, c % 2, u, :], ALU.mult).then_inc(mul_a, 1)

            def aux_out(item, n, b):
                kind, k = item[0], item[1]
                bank = aux(n)
                J = NPASS * b + k
                C = NC * b + k
                if kind == "max":
                    p = item[2]
                    dve.wait_ge(max_mm, J * MAXP + p + 1)
                    nc.vector.tensor_reduce(mpart[:, k % 2, p:p + 1], bank, AX_X, ALU.max).then_inc(max_red, 1)
                    if p == MAXP - 1:
                        dve.wait_ge(max_red, (J + 1) * MAXP)
                        dve.wait_ge(maxt_mm, LEAD + J)
                        nc.vector.tensor_reduce(m16[:, :], mpart[:, k % 2].rearrange("p (r k) -> p r k", k=4),
                                                AX_X, ALU.max).then_inc(m_ready, 1)
                elif kind == "max_t":
                    dve.wait_ge(maxt_mm, LEAD + J + 1)
                    if not isinstance(b, int) or b > 0 or k > 0:
                        dve.wait_ge(mrow_in[(k - 1) % 2], 32 * (NPASS // 2 * b + (k - 1) // 2 + 1))
                    nc.vector.tensor_scalar(mrow[:, 0, :], bank[0:4 * QT, 0:P], -1.0, None, ALU.mult
                                            ).then_inc(mhi, 1)
                    dve.wait_ge(mhi, J + 1)
                    nc.vector.scalar_tensor_tensor(mrow[:, 1, :], bank[0:4 * QT, 0:P], -1.0, mrow[:, 0, :],
                                                   ALU.mult, ALU.subtract).then_inc(maxt_cp, 1)
                elif kind == "den_t":
                    dve.wait_ge(dent_mm, J + 1)
                    nc.vector.reciprocal(rcp[:, :, :], bank.rearrange("p (t h r) -> p t h r", t=QT, h=4)[:, :, :, 0]
                                         ).then_inc(rcp_one, 1)
                    dve.wait_ge(rcp_one, J + 1)
                    nc.vector.tensor_copy(rcp32[:, :, :, :], rcp[:, :, :].unsqueeze(3).to_broadcast([P, QT, 4, HD])
                                          ).then_inc(rcp_done, 1)
                elif kind == "rden":
                    dve.wait_ge(rden_mm, J + 1)
                    nc.vector.tensor_tensor(attnT[:, k % HG, :], bank, attnT[:, k % HG, :], ALU.mult
                                            ).then_inc(attn_done, 1)
                elif kind == "proj":
                    t = item[2]
                    if t == 0:
                        dve.wait_ge(xb_done, C + 1)
                    dve.wait_ge(proj_mm, QT * C + t + 1)
                    nc.vector.tensor_tensor(y[:, t, :], bank[:, 0:D], y[:, t, :], ALU.add).then_inc(y_done, 1)
                    dve.wait_ge(y_done, LEAD + QT * C + t + 1)
                    nc.vector.bn_stats(stats[:, t, :], y[:, t, :]).then_inc(st_done, 1)
                    if t == QT - 1:
                        dve.wait_ge(st_done, QT * (C + 1))
                        dve.wait_ge(nmean_done, LEAD + C)
                        nc.vector.tensor_tensor(mv[:, 0, :], stats[:, :, 1], stats[:, :, 4], ALU.subtract)
                        nc.vector.tensor_tensor(mv[:, 1, :], stats[:, :, 1], stats[:, :, 4], ALU.add)
                        nc.vector.tensor_tensor(mv[:, 2, :], stats[:, :, 2], stats[:, :, 5], ALU.add
                                                ).then_inc(mv_one, 1)
                        dve.wait_ge(mv_one, C + 1)
                        nc.vector.scalar_tensor_tensor(mv[:, 3, :], mv[:, 0, :], 0.25, mv[:, 0, :], ALU.mult, ALU.mult)
                        nc.vector.tensor_scalar(mv[:, 4, :], mv[:, 1, :], -0.5, None, ALU.mult)
                        nc.vector.tensor_scalar(mv[:, 5, :], mv[:, 2, :], 1.0 / D, LN_EPS, ALU.mult, ALU.add
                                                ).then_inc(mv_two, 1)
                        dve.wait_ge(mv_two, C + 1)
                        nc.vector.tensor_tensor(mv[:, 6, :], mv[:, 3, :], mv[:, 5, :], ALU.add).then_inc(var_done, 1)

            for n, item in enumerate(prologue_items()):
                aux_out(item, n, 0)
            for u in range(LOOK):
                weights_a(0, 0, u)

            def attend_batch(b, last):
                n = 0
                for j in range(NPASS):
                    for u in range(KT):
                        ahead = divmod(KT * j + u + LOOK, KT)
                        items = aux_items(j, u, last)
                        cut = (len(items) * 3 + 3) // 4
                        for item in items[:cut]:
                            aux_out(item, n, b)
                            n += 1
                        if not (last and ahead[0] == NPASS):
                            weights_a(b, *ahead)
                        for item in items[cut:]:
                            aux_out(item, n, b)
                            n += 1
                for item in tail_items():
                    aux_out(item, n, b)
                    n += 1

            batches(dve, attend_batch)

        @block.gpsimd
        def _(pool):
            for done in (mul_b, nmean_done):
                pool.sem_inc(done, LEAD)
            nc.gpsimd.memset(ident[:, :], 0.0).then_inc(ident_zero, 1)
            nc.gpsimd.memset(ones_v[:, :], 1.0).then_inc(const_ready, 1)
            nc.gpsimd.memset(minus_half[:, :], -0.5).then_inc(const_ready, 1)
            pool.wait_ge(ident_zero, 1)
            nc.gpsimd.affine_select(out=ident[:, :], in_=ident[:, :], compare_op=ALU.not_equal, fill=1.0,
                                    base=0, pattern=[[-1, P]], channel_multiplier=1).then_inc(const_ready, 1)
            pool.wait_ge(const_ready, 3)
            nc.gpsimd.memset(kmain[KROWS:SROWS], 1.0).then_inc(k_ones, 1)
            pool.wait_ge(bo_ready, 16)

            def weights_b(b, j, u):
                U = NU * b + KT * j + u
                c, g = divmod(j, HG)
                if g == 0:
                    pool.wait_ge(adjt_cp, (NC * b + c) * KT + u + 1)
                pool.wait_ge(exp_b, HB * (U + 1))
                nc.gpsimd.tensor_tensor(pb[:, u % RING], pb[:, u % RING],
                                        adjT[:, c % 2, u, :].unsqueeze(1).to_broadcast([P, HB, QC]), ALU.mult
                                        ).then_inc(mul_b, 1)

            def add_bias(b, c):
                pool.wait_ge(xres_in, 16 * (NC * b + c + 1))
                nc.gpsimd.tensor_tensor(y[:, :, :], y[:, :, :],
                                        bo_b[:, :].unsqueeze(1).to_broadcast([P, QT, D]), ALU.add
                                        ).then_inc(xb_done, 1)

            def norm_scalars(b, c):
                C = NC * b + c
                pool.wait_ge(var_done, C + 1)
                pool.wait_ge(ln_done, LEAD + C)
                nc.gpsimd.tensor_tensor(rstd[:, :], mv[:, 6, :], minus_half[:, :], ALU.pow).then_inc(rstd_done, 1)
                pool.wait_ge(rstd_done, C + 1)
                nc.gpsimd.tensor_tensor(nmean[:, :], mv[:, 4, :], rstd[:, :], ALU.mult
                                        ).then_inc(nmean_done, 1)

            pool.sem_inc(pv_done, RING)
            weights_b(0, 0, 0)

            def attend_batch(b, last):
                for j in range(NPASS):
                    c, g = divmod(j, HG)
                    for u in range(KT):
                        if not (last and j == NPASS - 1 and u == KT - 1):
                            weights_b(b, *divmod(KT * j + u + 1, KT))
                        if g == 1 and u == 8:
                            add_bias(b, c)
                        if g == 0 and j >= 2 and u == 10:
                            norm_scalars(b, c - 1)
                norm_scalars(b, NC - 1)

            batches(pool, attend_batch)


_INS = ["x", "adj", "L0_gnn_Wq", "L0_gnn_Wk", "L0_gnn_Wv", "L0_gnn_Wo", "L0_gnn_bo"]


def kernel(**inputs):
    import numpy as _np
    import concourse.bacc as _bacc
    from concourse import mybir as _mybir
    from concourse.bass_utils import run_bass_kernel_spmd as _run

    nc = _bacc.Bacc("TRN2", target_bir_lowering=False, num_devices=1)
    arrays, args = {}, []
    for name in _INS:
        a = _np.ascontiguousarray(inputs[name])
        arrays[f"in_{name}"] = a
        args.append(nc.dram_tensor(f"in_{name}", a.shape, _mybir.dt.from_np(a.dtype), kind="ExternalInput").ap())
    out = nc.dram_tensor("out", (B, N, D), F32, kind="ExternalOutput")
    attention_layer(nc, *args, out.ap())
    r = _run(nc, [arrays], core_ids=[0])
    return r.results[0]["out"]
```
